# Optimizing a Trainium2 kernel written in Bass

```python
import numpy as np
import jax
import jax.numpy as jnp

def _softmax(x, axis=-1):
    return jax.nn.softmax(x, axis=axis)

def _gelu(x):
    return jax.nn.gelu(x, approximate=True)

def _silu(x):
    return jax.nn.silu(x)

def _sigmoid(x):
    return jax.nn.sigmoid(x)

def _layernorm(x, axis=-1, eps=1e-05):
    m = jnp.mean(x, axis=axis, keepdims=True)
    v = jnp.var(x, axis=axis, keepdims=True)
    return (x - m) / jnp.sqrt(v + eps)

def _scatter_add(tgt, idx, src, axis=0):
    return tgt.at[idx].add(src)

def _segment_sum(src, seg, n):
    return jax.ops.segment_sum(src, seg, n)
kernel_name = 'mk_gnn_preln_d1_gnn_r8_34202f'

def setup_inputs(seed: int=0):
    np.random.seed(seed)
    _w = jnp.asarray

    def _rec_inputs():
        import jax
        import jax.numpy as jnp
        _gk = jax.random.key(seed)
        x = -0.000202 + 1 * jax.random.normal(jax.random.fold_in(_gk, 1), (6250, 128), jnp.float32)
        _s = jax.random.randint(jax.random.fold_in(_gk, 2), (100000,), 0, 6250, jnp.int32)
        _d = jax.random.randint(jax.random.fold_in(_gk, 3), (100000,), 0, 6250, jnp.int32)
        _loop = jnp.arange(6250, dtype=jnp.int32)
        src = jnp.concatenate([_s, _d, _loop])
        dst = jnp.concatenate([_d, _s, _loop])
        _o = jnp.argsort(dst, stable=True)
        src = src[_o]
        dst = dst[_o]
        edge_attr_32 = 0.000103221 + 1.00003 * jax.random.normal(jax.random.fold_in(_gk, 12), (206250, 32), jnp.float32)
        edge_weight = jax.random.uniform(jax.random.fold_in(_gk, 13), (206250,), jnp.float32, 0.0, 1)
        return (x, src, dst, edge_attr_32, edge_weight)
    x, src, dst, edge_attr_32, edge_weight = _rec_inputs()

    def _L0_gnn_setup():
        import jax, jax.numpy as jnp
        import numpy as np
        N_NODES = 6250
        N_EDGES = 200000
        IN_CH = 128
        EDGE_DIM = 32
        OUT_CH = 128
        key = jax.random.key(seed)
        ks = jax.random.split(key, 6)
        x = jax.random.normal(ks[0], (N_NODES, IN_CH), dtype=jnp.float32)
        row = jax.random.randint(ks[1], (N_EDGES,), 0, N_NODES, dtype=jnp.int32)
        col = jax.random.randint(ks[2], (N_EDGES,), 0, N_NODES, dtype=jnp.int32)
        norm = jax.random.uniform(ks[3], (N_EDGES,), dtype=jnp.float32)
        edge_attr = jax.random.normal(ks[4], (N_EDGES, EDGE_DIM), dtype=jnp.float32)
        fan = IN_CH + EDGE_DIM + OUT_CH
        std = jnp.sqrt(6.0 / fan)
        W = jax.random.uniform(ks[5], (IN_CH + EDGE_DIM, OUT_CH), dtype=jnp.float32, minval=-std, maxval=std)
        b = jnp.zeros((OUT_CH,), dtype=jnp.float32)
        return {'x': x, 'row': row, 'col': col, 'norm': norm, 'edge_attr': edge_attr, 'W': W, 'b': b}
    _L0_gnn_all = _L0_gnn_setup()
    _L0_gnn_in = {k: v for k, v in _L0_gnn_all.items() if k in ('W', 'b')}
    del _L0_gnn_all
    return {'x': x, 'src': src, 'dst': dst, 'edge_attr_32': edge_attr_32, 'edge_weight': edge_weight, 'L0_gnn_W': _L0_gnn_in['W'], 'L0_gnn_b': _L0_gnn_in['b']}

def reference(x, src, dst, edge_attr_32, edge_weight, L0_gnn_W, L0_gnn_b):
    import jax
    import jax.numpy as jnp

    def _L0_gnn_ref(x, row, col, norm, edge_attr, W, b):
        import jax, jax.numpy as jnp
        import numpy as np
        N_NODES = 6250
        N_EDGES = 200000
        IN_CH = 128
        EDGE_DIM = 32
        OUT_CH = 128
        msg_x = norm[:, None] * x[col]
        agg = jax.ops.segment_sum(msg_x, row, num_segments=N_NODES)
        msg_e = norm[:, None] * edge_attr
        agg_e = jax.ops.segment_sum(msg_e, row, num_segments=N_NODES)
        out = jnp.concatenate([agg, agg_e], axis=1)
        return out @ W + b
    h = jnp.maximum(_layernorm(x, axis=-1), 0.0)
    x = x + _L0_gnn_ref(h, src, dst, edge_weight, edge_attr_32, L0_gnn_W, L0_gnn_b)
    return x

_drawn_inputs = setup_inputs


def setup_inputs(seed=0):
    import zlib

    import numpy as np

    out = dict(_drawn_inputs(seed))
    spreads = {'L0_gnn_b': (0.0, 0.541)}
    factors = {}
    for name, (base, spread) in spreads.items():
        noise = np.random.default_rng([zlib.crc32(name.encode()), seed]).standard_normal(out[name].shape)
        drawn = base * np.exp(spread * noise) if base else spread * noise
        out[name] = jnp.asarray(drawn.astype(out[name].dtype))
    for name, factor in factors.items():
        out[name] = (out[name] * factor).astype(out[name].dtype)
    return out
```

```python
from contextlib import ExitStack

import concourse.bass as bass
from concourse import mybir

ALU = mybir.AluOpType
ACT = mybir.ActivationFunctionType
AX = mybir.AxisListType
F32 = mybir.dt.float32
BF16 = mybir.dt.bfloat16
I32 = mybir.dt.int32

P = 128
TRIPLE = 3
CHUNKS = 12
TRIPLES = CHUNKS // TRIPLE
GROUP = CHUNKS * P
SLOTS = 3
TURN = SLOTS * TRIPLES
TABLES = 4
PIECES = 10
ROWS_RING = 6
LAG = 2
START = 8
NEVER = 8192


def gnn_kernel(nc, x, src, dst, edge_attr, edge_weight, W, b, out):
    N, F = x.shape
    E, D = edge_attr.shape
    WIN = P - D - 1
    ONE = WIN
    NG = -(-E // (GROUP * SLOTS)) * SLOTS
    TURNS = NG // SLOTS
    FULL = (NG - 1) * GROUP
    SHORT = -(-(E - FULL) // P)
    SPAN = SHORT * P
    PAD = FULL + SPAN - E
    NT = -(-N // P)
    NF = N // P
    NR = N - NF * P
    QUAD = 4
    QUADS = -(-NT // QUAD)
    WINDOWS = -(-N // WIN)
    G_ROWS = (NT + 1) * P
    G_ALL = -(-(N + WINDOWS * WIN) // P) * P
    C1 = F + 1
    assert F == P and D == 32 and 0 < SHORT <= CHUNKS and SPAN <= E and TURNS > 2
    assert CHUNKS * SLOTS % TABLES == 0 and TURN % ROWS_RING == 0

    tables = [nc.dram_tensor(f"table{r}", (N, F), F32).ap() for r in range(TABLES)]
    g_dram = nc.dram_tensor("g_rows", (G_ALL, F), F32).ap()
    w_last = nc.dram_tensor("weights_of_last_group", (SPAN,), F32).ap()
    hl_dram = nc.dram_tensor("src_high_low", (2, FULL + SPAN), BF16).ap()
    ends_dram = nc.dram_tensor("group_ends", (2, 2 * NG), I32).ap()

    ctx = ExitStack()
    with ctx:
        def sb(name, shape, dt):
            return ctx.enter_context(nc.sbuf_tensor(name, shape, dt))

        def bank(name):
            return ctx.enter_context(nc.psum_tensor(name, [P, 512], F32))

        def sem(name):
            return ctx.enter_context(nc.semaphore(name))

        cuts = [0, 4, 16, 32, NF]
        STEP = 6
        parts = [(t, min(t + STEP, NF), P) for t in range(0, NF, STEP)] + [(NF, NF + 1, NR)]

        ident = sb("ident", [P, P], F32)
        ones2 = sb("ones2", [2, P], BF16)
        slot_no = sb("slot_no", [P, WIN], I32)
        slot_nof = sb("slot_nof", [P, WIN], F32)
        power_i = sb("power_i", [P, 1], I32)
        power = power_i[:].bitcast(F32)
        limit = sb("limit", [P, 1], F32)
        part_no = sb("part_no", [P, 1], I32)
        one_row = sb("one_row", [P, 1], F32)
        ramp_i = sb("ramp_i", [1, WINDOWS], I32)
        live = sb("live", [P, 1], F32)
        x_sb = sb("x_sb", [P, NT, F], F32)
        xb_sb = sb("xb_sb", [P, NT, F], F32)
        b_sb = sb("b_sb", [P, F], F32)
        wx_sb = sb("wx_sb", [F, F], F32)
        stats = sb("stats", [P, NT, 6], F32)
        mv = sb("mv", [P, NT, 2], F32)
        minus_mean = sb("minus_mean", [P, NT], F32)
        var_eps = sb("var_eps", [P, NT], F32)
        sigma = sb("sigma", [P, NT], F32)
        rstd = sb("rstd", [P, NT], F32)
        h_sb = sb("h_sb", [P, NT, F], F32)
        hT_sb = sb("hT_sb", [P, 2, QUAD, P], F32)
        g_sb = sb("g_sb", [P, NT + 1, F], F32)
        zeros = sb("zeros", [P, N // PIECES], F32)
        SRC_ROW = (FULL + SPAN) // P
        src_all = sb("src_all", [P, SRC_ROW], I32)
        high_i = sb("high_i", [P, SRC_ROW], I32)
        high = sb("high", [P, SRC_ROW], BF16)
        low = sb("low", [P, SRC_ROW], BF16)
        HALF = GROUP // 2
        DP = 2 * NG // 3
        dst_all = sb("dst_all", [DP, 3, HALF], I32)
        ends = sb("ends", [DP, 2, 3], I32)
        ends_row = sb("ends_row", [1, 2, NG, 2], I32)
        ends_bc = sb("ends_bc", [P, NG, 2], I32)
        row_min = sb("row_min", [1, NG], I32)
        row_max = sb("row_max", [1, NG], I32)
        row_span = sb("row_span", [1, NG], I32)
        widest = sb("widest", [1, 1], F32)
        wider = sb("wider", [1, WINDOWS], F32)
        wider_n = sb("wider_n", [1, 1], F32)
        more_i = sb("more_i", [1, 1], I32)
        win_base = sb("win_base", [P, NG], F32)
        ea_sb = sb("ea_sb", [P, SLOTS, CHUNKS, D], F32)
        src_sb = sb("src_sb", [P, SLOTS, CHUNKS], I32)
        dst_sb = sb("dst_sb", [P, SLOTS, CHUNKS], I32)
        w_sb = sb("w_sb", [P, SLOTS, CHUNKS], F32)
        hl_sb = sb("hl_sb", [2, SLOTS, GROUP], BF16)
        G_sb = sb("G_sb", [P, SLOTS, C1], F32)
        q_sb = sb("q_sb", [P, SLOTS, CHUNKS], F32)
        X_sb = sb("X_sb", [P, SLOTS, CHUNKS, P], F32)
        S_sb = sb("S_sb", [P, 2, TRIPLE, P], F32)
        M_sb = sb("M_sb", [P, 2, TRIPLE, P], F32)
        rows_sb = sb("rows_sb", [P, ROWS_RING, TRIPLE, C1], F32)
        later = sb("later", [P, ROWS_RING, TRIPLE], F32)
        index = sb("index", [P, ROWS_RING, TRIPLE], I32)

        bc_ps = [bank(f"bc_ps{i}") for i in range(2)]
        M_ps = [bank(f"M_ps{i}") for i in range(2)]
        Y_ps = [bank(f"Y_ps{i}") for i in range(2)]
        g_ps = M_ps + Y_ps
        G_BANKS = len(g_ps)

        x_in = [sem(f"x_in{i}") for i in range(4)]
        wx_in = sem("wx_in")
        we_in = sem("we_in")
        b_in = sem("b_in")
        dst_in = sem("dst_in")
        src_in = sem("src_in")
        zeros_set = sem("zeros_set")
        const_set = sem("const_set")
        g_slots_set = sem("g_slots_set")
        x_tail_set = sem("x_tail_set")
        ends_set = sem("ends_set")
        ends_out = sem("ends_out")
        ends_in = sem("ends_in")
        chain = sem("chain")
        passes_set = sem("passes_set")
        high_i_set = sem("high_i_set")
        high_set = sem("high_set")
        low_set = sem("low_set")
        hl_out = sem("hl_out")
        w_out = sem("w_out")
        x_bias_set = sem("x_bias_set")
        slots_set = sem("slots_set")
        table_set = [sem(f"table_set{r}") for r in range(TABLES)]
        mean_set = sem("mean_set")
        var_set = sem("var_set")
        h_set = sem("h_set")
        sigma_set = sem("sigma_set")
        hT_ready = sem("hT_ready")
        hT_set = sem("hT_set")
        g_ready = sem("g_ready")
        g_set = sem("g_set")
        g_out = sem("g_out")
        past_out = sem("past_out")
        edges_in = [sem(f"edges_in{s}") for s in range(SLOTS)]
        window_in = [sem(f"window_in{s}") for s in range(SLOTS)]
        slot_taken = sem("slot_taken")
        q_set = sem("q_set")
        same_row = sem("same_row")
        same_set = sem("same_set")
        M_ready = sem("M_ready")
        M_set = sem("M_set")
        Y_ready = sem("Y_ready")
        rows_set = sem("rows_set")
        later_set = sem("later_set")
        index_set = sem("index_set")
        sent = sem("sent")
        table_done = [sem(f"table_done{r}") for r in range(TABLES)]
        live_cleared = sem("live_cleared")
        windows_moved = sem("windows_moved")
        pass_begun = sem("pass_begun")
        tables_over = sem("tables_over")
        counts_kept = sem("counts_kept")
        last_in = [sem(f"last_in{i}") for i in range(2)]
        sum_in = [sem(f"sum_in{i}") for i in range(len(parts))]
        sum_set = sem("sum_set")
        sum_chain = sem("sum_chain")
        sum_out = sem("sum_out")

        CONSTS = 6
        ALL_CONSTS = CONSTS + 2

        def part_of(t):
            return max(i for i in range(4) if cuts[i] <= t)

        def done(t):
            return t + 1 + START

        LAST = TABLES - 1

        ALL = SLOTS * CHUNKS
        LAST_ALL = ALL - CHUNKS + SHORT
        table_of = {"first": [*(c % LAST for c in range(ALL - 1)), LAST],
                    "middle": [c % TABLES for c in range(ALL)],
                    "last": [c % LAST for c in range(LAST_ALL)]}

        def count(r, kind, c=ALL):
            return table_of[kind][:c].count(r)

        def added(r, p, i, kind, c):
            if kind == "first":
                return count(r, kind, c)
            return (p + i) * count(r, "middle") + (count(r, "first") - count(r, "middle") + count(r, kind, c))

        def all_turns(eng, turn, after_first=None, before_more=None, next_pass=None):
            eng.wait_ge(passes_set, 1)
            more = eng.value_load(more_i[0:1, 0:1], min_val=0, max_val=WINDOWS - 1)
            turn(0, 0, 0, "first")
            if after_first:
                after_first()
            with eng.Fori(1, TURNS - 1) as i:
                turn(0, i, i, "middle")
            with eng.If(more > 0):
                if before_more:
                    before_more()
                with eng.Fori(0, more) as p:
                    turn(p, p * TURNS + (TURNS - 1), TURNS - 1, "last")
                    if next_pass:
                        next_pass(p + 1)
                    with eng.Fori(0, TURNS - 1) as i:
                        turn(p + 1, p * TURNS + i + TURNS, i, "middle")
            turn(more, more * TURNS + (TURNS - 1), TURNS - 1, "last")
            return more

        block = ctx.enter_context(nc.Block())

        def rows_of(a, t0, t1):
            return a[t0 * P:t1 * P, :].rearrange("(t p) f -> p t f", p=P)

        acc_in = [h_sb, xb_sb, g_sb, x_sb]
        HALF_CLEAR = PIECES // 2
        STARTS = [2, 2, 3, PIECES // 2]

        def load_part(sp, r, part, loaded):
            t0, t1, np_ = part
            to = acc_in[r][0:np_, t0:t1, :]
            if np_ == P:
                sp.dma_start(to, rows_of(tables[r], t0, t1)).then_inc(loaded, 16)
            else:
                sp.dma_start(to[:, 0, :], tables[r][NF * P:N, :]).then_inc(loaded, 16)

        def clear_table(eng, r, a, b):
            flat = tables[r].rearrange("n f -> (n f)").rearrange("(p h c) -> p h c", p=P, h=PIECES)
            eng.dma_start(flat[:, a:b, :], zeros[:].unsqueeze(1).to_broadcast([P, b - a, N // PIECES])).then_inc(table_set[r], 16)

        @block.sync
        def _(sp):
            for i in range(4):
                sp.dma_start(x_sb[:, cuts[i]:cuts[i + 1], :], rows_of(x, cuts[i], cuts[i + 1])).then_inc(x_in[i], 16)
                if i == 0:
                    sp.dma_start(wx_sb[:], W[0:F, :]).then_inc(wx_in, 16)
            sp.wait_ge(x_tail_set, 1)
            sp.dma_start(x_sb[0:NR, NF, :], x[NF * P:N, :]).then_inc(x_in[3], 16)
            sp.wait_ge(g_slots_set, 1)
            for s in range(SLOTS):
                sp.dma_start(G_sb[WIN + 1:P, s, 0:F], W[F:F + D, :]).then_inc(we_in, 16)
            def load_edges(s, group, short):
                k = SHORT if short else CHUNKS
                e0 = E - SPAN if short else group * GROUP
                for to, of in ((src_sb, src), (dst_sb, dst), (w_sb, edge_weight)):
                    some = w_last[:] if short and of is edge_weight else of[bass.ds(e0, k * P)]
                    sp.dma_start(to[:, s, 0:k], some.rearrange("(p k) -> p k", p=P)).then_inc(edges_in[s], 16)
                of = edge_attr[bass.ds(e0, k * P), :].rearrange("(p k) d -> p k d", p=P)
                sp.dma_start(ea_sb[:, s, 0:k, :], of).then_inc(edges_in[s], 16)

            def load_high_low(s, group, short):
                to, of = hl_sb[:, s, :], hl_dram[:, bass.ds(group * GROUP, SPAN if short else GROUP)]
                if short:
                    to = to.rearrange("r (p k) -> r p k", k=CHUNKS)[:, :, 0:SHORT]
                    of = of.rearrange("r (p k) -> r p k", k=SHORT)
                sp.dma_start(to, of).then_inc(edges_in[s], 16)

            sp.wait_ge(zeros_set, 1)
            clear_table(sp, 1, 0, HALF_CLEAR)
            clear_table(sp, 1, HALF_CLEAR, PIECES)
            sp.wait_ge(x_bias_set, 1)
            sp.dma_start(rows_of(tables[0], 0, NF), xb_sb[:, 0:NF, :]).then_inc(table_set[0], 16)
            sp.dma_start(tables[0][NF * P:N, :], xb_sb[0:NR, NF, :]).then_inc(table_set[0], 16)
            sp.wait_ge(ends_set, 1)
            for a in range(2):
                sp.dma_start(ends_dram[a, :].rearrange("(p s) -> p s", s=3), ends[:, a, :]).then_inc(ends_out, 16)
            clear_table(sp, 2, 0, HALF_CLEAR)
            load_edges(0, 0, False)
            sp.wait_ge(ends_out, 32)
            sp.dma_start(ends_row[:].rearrange("o a g h -> o (a g h)"), ends_dram.rearrange("a g -> (a g)")[None, :]).then_inc(ends_in, 16)
            sp.dma_start(ends_bc[:].rearrange("p g h -> p (g h)"), ends_dram[0, :].partition_broadcast(P)).then_inc(ends_in, 16)

            def store_g(i):
                t0, t1 = cuts[i], cuts[i + 1] if i < 3 else NT + 1
                sp.wait_ge(g_set, min(-(-t1 // QUAD), QUADS))
                sp.dma_start(rows_of(g_dram, t0, t1), g_sb[:, t0:t1, :]).then_inc(g_out, 16)

            store_g(0)
            store_g(1)
            sp.wait_ge(high_set, 1)
            sp.wait_ge(low_set, 1)
            for r, part in enumerate((high, low)):
                sp.dma_start(hl_dram[r, :].rearrange("(p c) -> p c", p=P), part[:]).then_inc(hl_out, 16)
            store_g(2)

            def window_base(group):
                return sp.value_load(row_min[0:1, bass.ds(group, 1)], min_val=0, max_val=N - 1)

            def load_window(s, base, p):
                sp.dma_start(G_sb[0:WIN, s, 0:F], g_dram[bass.ds(base + p * WIN, WIN), :]).then_inc(window_in[s], 16)

            def turn(p, n, i, kind):
                if kind == "first":
                    sp.wait_ge(hl_out, 32)
                    load_high_low(0, 0, False)
                    store_g(3)
                    clear_table(sp, 2, HALF_CLEAR, HALF_CLEAR + 2)
                    bases = [window_base(s) for s in range(SLOTS)]
                    sp.wait_ge(g_out, 64)
                    load_window(0, bases[0], 0)
                    clear_table(sp, 2, HALF_CLEAR + 2, PIECES)
                    for s in range(1, SLOTS):
                        load_edges(s, s, False)
                        load_high_low(s, s, False)
                        load_window(s, bases[s], 0)
                    return
                if kind == "last":
                    sp.wait_ge(w_out, 32)
                for s in range(SLOTS):
                    group = i * SLOTS + s
                    sp.wait_ge(index_set, done(n * TURN - TURN + s * TRIPLES + TRIPLES - 1))
                    sp.sem_inc(slot_taken, 1)
                    short = kind == "last" and s == SLOTS - 1
                    load_edges(s, group, short)
                    load_high_low(s, group, short)
                    load_window(s, window_base(group), p)

            def after_first():
                for i, a in enumerate(range(0, PIECES, 2)):
                    if i:
                        sp.wait_ge(table_set[LAST], 16 * i)
                    clear_table(sp, LAST, a, a + 2)

            def clear_past_end():
                most = zeros.shape[1] // F
                cut = [*range(G_ROWS, G_ALL, most * P), G_ALL]
                for a0, a1 in zip(cut, cut[1:]):
                    sp.dma_start(g_dram[a0:a1, :].rearrange("(p c) f -> p (c f)", p=P), zeros[:, 0:(a1 - a0) // P * F]).then_inc(past_out, 16)
                sp.wait_ge(past_out, 16 * (len(cut) - 1))

            def next_pass(p):
                sp.wait_ge(counts_kept, p)
                sp.sem_inc(slot_taken, 1)

            more = all_turns(sp, turn, after_first, clear_past_end, next_pass)

            for r in (LAST, *range(LAST)):
                sp.wait_ge(table_done[r], added(r, more, TURNS - 1, "last", LAST_ALL) * 16)
                sp.sem_inc(tables_over, 1)
                if r == LAST:
                    for i, part in enumerate(parts):
                        if i >= 2:
                            sp.wait_ge(last_in[i % 2], 16 * (i // 2))
                        load_part(sp, r, part, last_in[i % 2])
            for part, loaded in zip(parts, sum_in):
                for r in range(LAST):
                    load_part(sp, r, part, loaded)

        @block.scalar
        def _(act):
            flat = dst_all[:].rearrange("p s c -> p (s c)")
            row = 3 * HALF
            most = 80
            act.dma_start(b_sb[:], b.partition_broadcast(P)).then_inc(b_in, 16)
            act.dma_start(flat[0:most, :], dst[0:most * row].rearrange("(p c) -> p c", c=row)).then_inc(dst_in, 16)
            act.dma_start(flat[most:DP - 1, :], dst[most * row:(DP - 1) * row].rearrange("(p c) -> p c", c=row)).then_inc(dst_in, 16)
            act.dma_start(flat[DP - 1:DP, 0:HALF], dst[None, (DP - 1) * row:FULL]).then_inc(dst_in, 16)
            act.dma_start(flat[DP - 1:DP, HALF:row], dst[None, E - GROUP:E]).then_inc(dst_in, 16)
            row = SRC_ROW
            most = 112
            act.dma_start(src_all[0:most, :], src[0:most * row].rearrange("(p c) -> p c", c=row)).then_inc(src_in, 16)
            act.dma_start(src_all[most:P - 1, :], src[most * row:(P - 1) * row].rearrange("(p c) -> p c", c=row)).then_inc(src_in, 16)
            act.dma_start(src_all[P - 1:P, 0:row - SPAN], src[None, (P - 1) * row:FULL]).then_inc(src_in, 16)
            act.dma_start(src_all[P - 1:P, row - SPAN:row], src[None, E - SPAN:E]).then_inc(src_in, 16)
            act.dma_start(w_last[None, PAD:SPAN], edge_weight[None, FULL:E]).then_inc(w_out, 16)
            act.wait_ge(zeros_set, 1)
            act.dma_start(w_last[None, 0:PAD], zeros[0:1, 0:PAD]).then_inc(w_out, 16)

            def make_h(q):
                t0, t1 = q * QUAD, min(q * QUAD + QUAD, NT)
                act.wait_ge(mean_set, part_of(t0) + 1)
                for t in range(t0, t1):
                    last = act.activation(h_sb[:, t, :], x_sb[:, t, :], ACT.Relu, bias=minus_mean[:, t:t + 1])
                last.then_inc(h_set, 1)

            def copy_hT(q):
                n = min(QUAD, NT - q * QUAD)
                act.wait_ge(hT_ready, q + 1)
                if q >= 2:
                    act.wait_ge(g_ready, q - 1)
                act.copy(hT_sb[:, q % 2, 0:n, :], bc_ps[q % 2][:, 0:n * P].rearrange("p (t c) -> p t c", c=P)).then_inc(hT_set, 1)

            for q in range(QUADS):
                if q == G_BANKS:
                    act.wait_ge(var_set, 1)
                    act.sqrt(sigma[:], var_eps[:]).then_inc(sigma_set, 1)
                if q == QUADS // 2:
                    act.wait_ge(high_i_set, 1)
                    act.copy(high[:], high_i[:]).then_inc(high_set, 1)
                make_h(q)
                if q >= 1:
                    copy_hT(q - 1)
            copy_hT(QUADS - 1)
            act.sem_inc(M_set, START)
            act.sem_inc(rows_set, START)

            def copy_M(t, u):
                act.wait_ge(M_ready, done(t))
                act.wait_ge(Y_ready, done(t - 2))
                act.copy(M_sb[:, u % 2].rearrange("p k c -> p (k c)"), M_ps[u % 2][:, 0:TRIPLE * P]).then_inc(M_set, 1)

            def copy_rows(t, u):
                act.wait_ge(Y_ready, done(t))
                act.wait_ge(sent, done(t - ROWS_RING + 2))
                act.copy(rows_sb[:, u % ROWS_RING].rearrange("p k c -> p (k c)"), Y_ps[u % 2][:, 0:TRIPLE * C1]).then_inc(rows_set, 1)

            def turn(p, n, i, kind):
                for u in range(TURN):
                    t = n * TURN + u
                    copy_M(t, u)
                    if not (kind == "first" and u == 0):
                        copy_rows(t - 1, (u - 1) % TURN)

            more = all_turns(act, turn)
            copy_rows(more * (TURNS * TURN) + (TURNS * TURN - 1), TURN - 1)

            for i, (t0, t1, np_) in enumerate(parts):
                act.wait_ge(sum_set, i + 1)
                of = acc_in[LAST][0:np_, t0:t1, :]
                if np_ == P:
                    act.dma_start(rows_of(out, t0, t1), of).then_inc(sum_out, 16)
                else:
                    act.dma_start(out[NF * P:N, :], of[:, 0, :]).then_inc(sum_out, 16)
            act.wait_ge(sum_out, 16 * len(parts))

        @block.gpsimd
        def _(pool):
            pool.memset(x_sb[:, NF, :], 0.0).then_inc(x_tail_set, 1)
            pool.memset(ident[:], 0.0).then_inc(const_set, 1)
            pool.iota(slot_no[:], [[1, WIN]], base=0, channel_multiplier=0).then_inc(const_set, 1)
            pool.iota(power_i[:], [[1, 1]], base=(127 + 63) << 23, channel_multiplier=-(1 << 23)).then_inc(const_set, 1)
            pool.iota(part_no[:], [[1, 1]], base=0, channel_multiplier=1).then_inc(const_set, 1)
            pool.iota(ramp_i[:], [[WIN, WINDOWS]], base=WIN, channel_multiplier=0).then_inc(const_set, 1)
            pool.memset(live[:], 1.0).then_inc(const_set, 1)
            pool.memset(G_sb[:], 0.0).then_inc(g_slots_set, 1)
            pool.wait_ge(const_set, CONSTS)
            pool.affine_select(out=ident[:], in_=ident[:], compare_op=ALU.not_equal, fill=1.0, base=0, pattern=[[-1, P]], channel_multiplier=1).then_inc(const_set, 1)
            pool.memset(ones2[:], 1.0).then_inc(const_set, 1)
            pool.memset(zeros[:], 0.0).then_inc(zeros_set, 1)
            pool.memset(g_sb[:, NT, :], 0.0).then_inc(g_slots_set, 1)
            pool.wait_ge(b_in, 16)
            for i in range(4):
                pool.wait_ge(x_in[i], 16 + 16 * (i == 3))
                t0, t1 = cuts[i], cuts[i + 1] + (i == 3)
                last = pool.tensor_tensor(xb_sb[:, t0:t1, :], x_sb[:, t0:t1, :], b_sb[:].unsqueeze(1).to_broadcast([P, t1 - t0, F]), ALU.add)
            last.then_inc(x_bias_set, 1)
            pool.sem_inc(sent, START)

            bound = pool.alloc_register("last_row")

            def turn(p, n, i, kind):
                for u in range(TURN):
                    t = n * TURN + u
                    for k in range(TRIPLE):
                        c = u * TRIPLE + k
                        if c >= len(table_of[kind]):
                            break
                        r = table_of[kind][c]
                        if kind == "first" and r not in table_of[kind][:c]:
                            pool.wait_ge(table_set[r], 16 * STARTS[r])
                        else:
                            pool.wait_ge(table_done[r], added(r, p, i, kind, c) * 16)
                        if k == 0:
                            pool.wait_ge(index_set, done(t))
                        over = k == TRIPLE - 1 or c == len(table_of[kind]) - 1
                        pool.reg_alu(bound, pool.zero_reg, N - 1, ALU.add)
                        pool.indirect_dma_start(
                            tables[r], bass.IndirectOffsetOnAxis(index[:, u % ROWS_RING, k:k + 1], 0),
                            rows_sb[:, u % ROWS_RING, k, 0:F], None, bounds_check=bound, oob_is_err=False,
                            compute_op=ALU.add, engine_sem=sent if over else None).then_inc(table_done[r], 16)

            def next_pass(p):
                missing = (CHUNKS - SHORT) // TRIPLE
                pool.wait_ge(sent, done(p * (TURNS * TURN) - 1 - missing))
                for r in range(TABLES):
                    pool.wait_ge(table_done[r], added(r, p, TURNS - 2, "last", ALL) * 16)
                pool.sem_inc(sent, missing)
                dropped = [(TURNS - 2) * count(r, "middle") + count(r, "last") for r in range(TABLES)]
                pool.inc_swdge_sem(table_done, [16 * n for n in dropped], mode="sub")
                pool.sem_inc(counts_kept, 1)

            all_turns(pool, turn, next_pass=next_pass)

        @block.vector
        def _(dve):
            steps_done = [0]

            def small(ins):
                steps_done[0] += 1
                ins.then_inc(chain, 1)
                dve.wait_ge(chain, steps_done[0])

            dve.wait_ge(const_set, CONSTS)
            dve.tensor_copy(slot_nof[:], slot_no[:])
            dve.tensor_scalar(limit[:], power, 2.5, None, ALU.mult)
            small(dve.tensor_scalar(one_row[:], part_no[:], float(ONE), None, ALU.is_equal))
            dve.wait_ge(g_slots_set, 1)
            dve.tensor_copy(X_sb[:, :, :, ONE].rearrange("p s k -> p (s k)"), power.to_broadcast([P, SLOTS * CHUNKS]))
            dve.tensor_copy(G_sb[:, :, F], one_row[:].to_broadcast([P, SLOTS])).then_inc(slots_set, 1)

            for i in range(4):
                dve.wait_ge(x_in[i], 16 + 16 * (i == 3))
                tiles = range(cuts[i], cuts[i + 1] + (i == 3))
                for t in tiles:
                    last = dve.bn_stats(stats[:, t, :], x_sb[:, t, :])
                small(last)
                for t in tiles:
                    last = dve.bn_aggr(mv[:, t, :], stats[:, t, :])
                small(last)
                dve.tensor_scalar(minus_mean[:, tiles[0]:tiles[-1] + 1], mv[:, tiles[0]:tiles[-1] + 1, 0], -1.0, None, ALU.mult).then_inc(mean_set, 1)
            dve.tensor_scalar(var_eps[:], mv[:, :, 1], 1e-5, None, ALU.add).then_inc(var_set, 1)

            def least_and_greatest():
                dve.wait_ge(dst_in, 64)
                dve.tensor_reduce(ends[:, 0, :], dst_all[:], AX.X, ALU.min)
                dve.tensor_reduce(ends[:, 1, :], dst_all[:], AX.X, ALU.max).then_inc(ends_set, 1)

            def high_and_low():
                dve.wait_ge(src_in, 64)
                dve.tensor_scalar(high_i[:], src_all[:], -P, None, ALU.bitwise_and).then_inc(high_i_set, 1)
                dve.wait_ge(high_i_set, 1)
                dve.tensor_tensor(low[:], src_all[:], high_i[:], ALU.subtract).then_inc(low_set, 1)

            def scale_g(q):
                n = min(QUAD, NT - q * QUAD)
                t0 = q * QUAD
                dve.wait_ge(g_ready, q + 1)
                dve.tensor_tensor(g_sb[:, t0:t0 + n, :], g_ps[q % G_BANKS][:, 0:n * P].rearrange("p (t c) -> p t c", c=P),
                                  rstd[:, t0:t0 + n].unsqueeze(2).to_broadcast([P, n, F]), ALU.mult).then_inc(g_set, 1)

            high_and_low()
            dve.wait_ge(sigma_set, 1)
            small(dve.reciprocal(rstd[:], sigma[:]))
            for q in range(QUADS):
                if q == G_BANKS:
                    least_and_greatest()
                scale_g(q)

            dve.wait_ge(ends_in, 32)
            dve.tensor_tensor(row_min[:], ends_row[:, 0, :, 0], ends_row[:, 0, :, 1], ALU.min)
            small(dve.tensor_tensor(row_max[:], ends_row[:, 1, :, 0], ends_row[:, 1, :, 1], ALU.max))
            dve.tensor_tensor(win_base[:], ends_bc[:, :, 0], ends_bc[:, :, 1], ALU.min)
            small(dve.tensor_tensor(row_span[:], row_max[:], row_min[:], ALU.subtract))
            small(dve.tensor_reduce(widest[:], row_span[:], AX.X, ALU.max))
            small(dve.tensor_scalar(wider[:], ramp_i[:], widest[:, 0:1], None, ALU.is_le))
            small(dve.tensor_reduce(wider_n[:], wider[:], AX.X, ALU.add))
            dve.tensor_copy(more_i[:], wider_n[:]).then_inc(passes_set, 1)
            dve.sem_inc(same_set, START)
            dve.sem_inc(index_set, START)
            dve.sem_inc(later_set, START)

            def prepare(p, i, n, s):
                group = i * SLOTS + s
                whole = n * SLOTS + s
                dve.wait_ge(edges_in[s], (n + 1) * (5 * 16))
                dve.tensor_scalar(q_sb[:, s, :], dst_sb[:, s, :], win_base[:, bass.ds(group, 1)], None, ALU.subtract).then_inc(q_set, 1)
                dve.scalar_tensor_tensor(X_sb[:, s, :, WIN + 1:P], ea_sb[:, s, :, :], live[:, 0:1],
                                         w_sb[:, s, :].unsqueeze(2).to_broadcast([P, CHUNKS, D]), ALU.mult, ALU.mult)
                dve.wait_ge(q_set, whole + 1)

            def make_X_S(t, u):
                s, v = u // TRIPLES, u % TRIPLES
                for k in range(TRIPLE * v, TRIPLE * v + TRIPLE):
                    dve.tensor_scalar(X_sb[:, s, k, 0:WIN], slot_nof[:], q_sb[:, s, k:k + 1], w_sb[:, s, k:k + 1], ALU.is_equal, ALU.mult)
                dve.wait_ge(same_row, done(t))
                dve.wait_ge(M_ready, done(t - 2))
                dve.tensor_tensor(S_sb[:, u % 2], bc_ps[u % 2][:, 0:TRIPLE * P].rearrange("p (k c) -> p k c", c=P),
                                  src_sb[:, s, TRIPLE * v:TRIPLE * v + TRIPLE].unsqueeze(2).to_broadcast([P, TRIPLE, P]),
                                  ALU.is_equal).then_inc(same_set, 1)

            def make_index(t, u):
                s, v = u // TRIPLES, u % TRIPLES
                o = u % ROWS_RING
                dve.wait_ge(rows_set, done(t))
                dve.tensor_scalar(later[:, o, :], rows_sb[:, o, :, F], limit[:, 0:1], float(NEVER), ALU.is_gt, ALU.mult).then_inc(later_set, 1)
                dve.wait_ge(later_set, done(t))
                dve.tensor_tensor(index[:, o, :], later[:, o, :], src_sb[:, s, TRIPLE * v:TRIPLE * v + TRIPLE], ALU.add).then_inc(index_set, 1)

            def turn(p, n, i, kind):
                for u in range(TURN):
                    t = n * TURN + u
                    if u % TRIPLES == 0:
                        prepare(p, i, n, u // TRIPLES)
                    make_X_S(t, u)
                    if not (kind == "first" and u < LAG):
                        make_index(t - LAG, (u - LAG) % TURN)

            def next_pass(p):
                dve.memset(live[:], 0.0).then_inc(live_cleared, 1)
                dve.wait_ge(live_cleared, p)
                dve.tensor_scalar(win_base[:], win_base[:], float(WIN), None, ALU.add).then_inc(windows_moved, 1)
                dve.wait_ge(windows_moved, p)
                dve.sem_inc(pass_begun, 1)

            more = all_turns(dve, turn, next_pass=next_pass)
            for u in range(TURN - LAG, TURN):
                make_index(more * (TURNS * TURN) + (TURNS * TURN - TURN + u), u)

            for i in range(2):
                dve.wait_ge(last_in[i], 16 * ((len(parts) + 1 - i) // 2))
            for i, (t0, t1, np_) in enumerate(parts):
                dve.wait_ge(sum_in[i], 16 * LAST)
                acc = [a[0:np_, t0:t1, :] for a in acc_in]
                for r in range(LAST - 1):
                    dve.tensor_tensor(acc[LAST], acc[LAST], acc[r], ALU.add).then_inc(sum_chain, 1)
                    dve.wait_ge(sum_chain, i * (LAST - 1) + r + 1)
                dve.tensor_tensor(acc[LAST], acc[LAST], acc[LAST - 1], ALU.add).then_inc(sum_set, 1)

        @block.tensor
        def _(pe):
            pe.wait_ge(const_set, ALL_CONSTS)
            pe.wait_ge(wx_in, 16)

            def project(q):
                n = min(QUAD, NT - q * QUAD)
                pe.wait_ge(hT_set, q + 1)
                if q >= G_BANKS:
                    pe.wait_ge(g_set, q - G_BANKS + 1)
                for t in range(n):
                    last = pe.matmul(g_ps[q % G_BANKS][:, t * P:(t + 1) * P], hT_sb[:, q % 2, t, :], wx_sb[:], start=True, stop=True)
                last.then_inc(g_ready, 1)

            for q in range(QUADS):
                n = min(QUAD, NT - q * QUAD)
                pe.wait_ge(h_set, q + 1)
                if q >= 2:
                    pe.wait_ge(hT_set, q - 1)
                for t in range(n):
                    last = pe.transpose(bc_ps[q % 2][:, t * P:(t + 1) * P], h_sb[:, q * QUAD + t, :], ident[:])
                last.then_inc(hT_ready, 1)
                if q >= 1:
                    project(q - 1)
            project(QUADS - 1)
            pe.sem_inc(same_row, START)
            pe.sem_inc(M_ready, START)
            pe.sem_inc(Y_ready, START)
            pe.wait_ge(g_set, QUADS)
            pe.wait_ge(slots_set, 1)
            pe.wait_ge(we_in, 16 * SLOTS)

            def spread(t, u, n):
                s, v = u // TRIPLES, u % TRIPLES
                if v == 0:
                    pe.wait_ge(edges_in[s], (n + 1) * (5 * 16))
                pe.wait_ge(same_set, done(t - 2))
                hl = hl_sb[:, s, :].rearrange("r (p k) -> r k p", k=CHUNKS)[:, TRIPLE * v:TRIPLE * v + TRIPLE, :]
                pe.matmul(bc_ps[u % 2][:, 0:TRIPLE * P].rearrange("p (k c) -> p k c", c=P), ones2[:], hl, start=True, stop=True).then_inc(same_row, 1)

            def sum_same(t, u):
                s, v = u // TRIPLES, u % TRIPLES
                pe.wait_ge(same_set, done(t))
                pe.wait_ge(M_set, done(t - 2))
                for k in range(TRIPLE):
                    last = pe.matmul(M_ps[u % 2][:, k * P:(k + 1) * P], X_sb[:, s, TRIPLE * v + k, :], S_sb[:, u % 2, k, :], start=True, stop=True)
                last.then_inc(M_ready, 1)

            def messages(t, u, n):
                s = u // TRIPLES
                if u % TRIPLES == 0:
                    pe.wait_ge(window_in[s], (n + 1) * 16)
                pe.wait_ge(M_set, done(t))
                pe.wait_ge(rows_set, done(t - 2))
                for k in range(TRIPLE):
                    last = pe.matmul(Y_ps[u % 2][:, k * C1:(k + 1) * C1], M_sb[:, u % 2, k, :], G_sb[:, s, :], start=True, stop=True)
                last.then_inc(Y_ready, 1)

            def turn(p, n, i, kind):
                for u in range(TURN):
                    t = n * TURN + u
                    spread(t, u, n)
                    if not (kind == "first" and u < 1):
                        sum_same(t - 1, (u - 1) % TURN)
                    if not (kind == "first" and u < 2):
                        messages(t - 2, (u - 2) % TURN, n - (u < 2))

            more = all_turns(pe, turn)
            n = more * TURNS + (TURNS - 1)
            t = n * TURN + (TURN - 1)
            sum_same(t, TURN - 1)
            messages(t - 1, TURN - 2, n)
            messages(t, TURN - 1, n)


_INS = ["x", "src", "dst", "edge_attr_32", "edge_weight", "L0_gnn_W", "L0_gnn_b"]
_OUTS = [((6250, 128), "float32")]


def kernel(**inputs):
    import numpy as _np
    import concourse.bacc as _bacc
    from concourse import mybir as _mybir
    from concourse.bass_utils import run_bass_kernel_spmd as _run

    nc = _bacc.Bacc("TRN2", target_bir_lowering=False, num_devices=1)
    arrays, args = {}, []
    for name in _INS:
        a = _np.ascontiguousarray(inputs[name])
        arrays[f"in_{name}_dram"] = a
        args.append(nc.dram_tensor(f"in_{name}_dram", a.shape, _mybir.dt.from_np(a.dtype), kind="ExternalInput").ap())
    for i, (shape, dtype) in enumerate(_OUTS):
        dt = _mybir.dt.from_np(_np.dtype(dtype))
        args.append(nc.dram_tensor(f"out_{i}_dram", shape, dt, kind="ExternalOutput").ap())
    gnn_kernel(nc, *args)
    r = _run(nc, [arrays], core_ids=[0])
    return r.results[0]["out_0_dram"]
```
